# Optimizing a Trainium2 kernel written in Bass

```python
import numpy as np
import jax
import jax.numpy as jnp

def _softmax(x, axis=-1):
    return jax.nn.softmax(x, axis=axis)

def _gelu(x):
    return jax.nn.gelu(x, approximate=True)

def _silu(x):
    return jax.nn.silu(x)

def _sigmoid(x):
    return jax.nn.sigmoid(x)

def _layernorm(x, axis=-1, eps=1e-05):
    m = jnp.mean(x, axis=axis, keepdims=True)
    v = jnp.var(x, axis=axis, keepdims=True)
    return (x - m) / jnp.sqrt(v + eps)

def _scatter_add(tgt, idx, src, axis=0):
    return tgt.at[idx].add(src)

def _segment_sum(src, seg, n):
    return jax.ops.segment_sum(src, seg, n)
kernel_name = 'mk_gnn_preln_d2_gnn_r32_f38aaf'

def setup_inputs(seed: int=0):
    np.random.seed(seed)
    _w = jnp.asarray

    def _rec_inputs():
        import jax
        import jax.numpy as jnp
        _gk = jax.random.key(seed)
        x = -0.000202 + 1 * jax.random.normal(jax.random.fold_in(_gk, 1), (3125, 64), jnp.float32)
        _s = jax.random.randint(jax.random.fold_in(_gk, 2), (50000,), 0, 3125, jnp.int32)
        _d = jax.random.randint(jax.random.fold_in(_gk, 3), (50000,), 0, 3125, jnp.int32)
        _loop = jnp.arange(3125, dtype=jnp.int32)
        src = jnp.concatenate([_s, _d, _loop])
        dst = jnp.concatenate([_d, _s, _loop])
        _o = jnp.argsort(dst, stable=True)
        src = src[_o]
        dst = dst[_o]
        edge_attr_64 = -8.16379e-05 + 0.999858 * jax.random.normal(jax.random.fold_in(_gk, 12), (103125, 64), jnp.float32)
        return (x, src, dst, edge_attr_64)
    x, src, dst, edge_attr_64 = _rec_inputs()

    def _L0_gnn_setup():
        import jax, jax.numpy as jnp
        import numpy as np
        BN_EPS = 1e-05

        def _batchnorm(x, gamma, beta):
            m = jnp.mean(x, axis=0)
            v = jnp.var(x, axis=0)
            return (x - m) * jax.lax.rsqrt(v + BN_EPS) * gamma + beta
        N, E, D = (3125, 50000, 64)
        key = jax.random.key(seed)
        ks = jax.random.split(key, 6)
        return {'node_feats': jax.random.normal(ks[0], (N, D), dtype=jnp.float32), 'edge_feats': jax.random.normal(ks[1], (E, D), dtype=jnp.float32), 'src': jax.random.randint(ks[2], (E,), 0, N, dtype=jnp.int32), 'dst': jax.random.randint(ks[3], (E,), 0, N, dtype=jnp.int32), 'eps': jnp.zeros((1,), dtype=jnp.float32), 'W1': jax.random.normal(ks[4], (D, 2 * D), dtype=jnp.float32) * (1.0 / np.sqrt(D)), 'b1': jnp.zeros((2 * D,), dtype=jnp.float32), 'gamma1': jnp.ones((2 * D,), dtype=jnp.float32), 'beta1': jnp.zeros((2 * D,), dtype=jnp.float32), 'W2': jax.random.normal(ks[5], (2 * D, D), dtype=jnp.float32) * (1.0 / np.sqrt(2 * D)), 'b2': jnp.zeros((D,), dtype=jnp.float32), 'gamma2': jnp.ones((D,), dtype=jnp.float32), 'beta2': jnp.zeros((D,), dtype=jnp.float32)}
    _L0_gnn_all = _L0_gnn_setup()
    _L0_gnn_in = {k: v for k, v in _L0_gnn_all.items() if k in ('eps', 'W1', 'b1', 'gamma1', 'beta1', 'W2', 'b2', 'gamma2', 'beta2')}
    del _L0_gnn_all

    def _L1_gnn_setup():
        import jax, jax.numpy as jnp
        import numpy as np
        N_NODES = 3125
        N_CHANNELS = 64
        N_EDGES = 37500
        K_CHEB = 6

        def _cheb_norm(edge_index, num_nodes):
            row, col = (edge_index[0], edge_index[1])
            ones = jnp.ones(edge_index.shape[1], dtype=jnp.float32)
            deg = jax.ops.segment_sum(ones, row, num_segments=num_nodes)
            dinv = jnp.where(deg > 0, jax.lax.rsqrt(jnp.where(deg > 0, deg, 1.0)), 0.0)
            norm = -dinv[row] * dinv[col]
            return norm

        def _propagate(x, row, col, norm, num_nodes):
            msgs = norm[:, None] * x[col]
            return jax.ops.segment_sum(msgs, row, num_segments=num_nodes)

        def _cheb_conv(x, W, b, row, col, norm, num_nodes):
            Tx0 = x
            out = Tx0 @ W[0]
            Tx1 = _propagate(Tx0, row, col, norm, num_nodes)
            out = out + Tx1 @ W[1]
            for k in range(2, W.shape[0]):
                Tx2 = 2.0 * _propagate(Tx1, row, col, norm, num_nodes) - Tx0
                out = out + Tx2 @ W[k]
                Tx0, Tx1 = (Tx1, Tx2)
            return out + b
        key = jax.random.key(seed)
        ks = jax.random.split(key, 8)
        pos = jax.random.normal(ks[0], (N_NODES, N_CHANNELS), dtype=jnp.float32)
        edge_index = jax.random.randint(ks[1], (2, N_EDGES), 0, N_NODES, dtype=jnp.int64)
        scale = 1.0 / np.sqrt(N_CHANNELS)
        W1 = jax.random.normal(ks[2], (K_CHEB, N_CHANNELS, N_CHANNELS), dtype=jnp.float32) * scale
        W2 = jax.random.normal(ks[3], (K_CHEB, N_CHANNELS, N_CHANNELS), dtype=jnp.float32) * scale
        W3 = jax.random.normal(ks[4], (K_CHEB, N_CHANNELS, N_CHANNELS), dtype=jnp.float32) * scale
        b1 = jnp.zeros((N_CHANNELS,), dtype=jnp.float32)
        b2 = jnp.zeros((N_CHANNELS,), dtype=jnp.float32)
        b3 = jnp.zeros((N_CHANNELS,), dtype=jnp.float32)
        return {'pos': pos, 'edge_index': edge_index, 'W1': W1, 'b1': b1, 'W2': W2, 'b2': b2, 'W3': W3, 'b3': b3}
    _L1_gnn_all = _L1_gnn_setup()
    _L1_gnn_in = {k: v for k, v in _L1_gnn_all.items() if k in ('W1', 'b1', 'W2', 'b2', 'W3', 'b3')}
    del _L1_gnn_all
    return {'x': x, 'src': src, 'dst': dst, 'edge_attr_64': edge_attr_64, 'L0_gnn_eps': _L0_gnn_in['eps'], 'L0_gnn_W1': _L0_gnn_in['W1'], 'L0_gnn_b1': _L0_gnn_in['b1'], 'L0_gnn_gamma1': _L0_gnn_in['gamma1'], 'L0_gnn_beta1': _L0_gnn_in['beta1'], 'L0_gnn_W2': _L0_gnn_in['W2'], 'L0_gnn_b2': _L0_gnn_in['b2'], 'L0_gnn_gamma2': _L0_gnn_in['gamma2'], 'L0_gnn_beta2': _L0_gnn_in['beta2'], 'L1_gnn_W1': _L1_gnn_in['W1'], 'L1_gnn_b1': _L1_gnn_in['b1'], 'L1_gnn_W2': _L1_gnn_in['W2'], 'L1_gnn_b2': _L1_gnn_in['b2'], 'L1_gnn_W3': _L1_gnn_in['W3'], 'L1_gnn_b3': _L1_gnn_in['b3']}

def reference(x, src, dst, edge_attr_64, L0_gnn_eps, L0_gnn_W1, L0_gnn_b1, L0_gnn_gamma1, L0_gnn_beta1, L0_gnn_W2, L0_gnn_b2, L0_gnn_gamma2, L0_gnn_beta2, L1_gnn_W1, L1_gnn_b1, L1_gnn_W2, L1_gnn_b2, L1_gnn_W3, L1_gnn_b3):
    import jax
    import jax.numpy as jnp

    def _L0_gnn_ref(node_feats, edge_feats, src, dst, eps, W1, b1, gamma1, beta1, W2, b2, gamma2, beta2):
        import jax, jax.numpy as jnp
        import numpy as np
        BN_EPS = 1e-05

        def _batchnorm(x, gamma, beta):
            m = jnp.mean(x, axis=0)
            v = jnp.var(x, axis=0)
            return (x - m) * jax.lax.rsqrt(v + BN_EPS) * gamma + beta
        N = node_feats.shape[0]
        msg = node_feats[src] + edge_feats
        agg_sum = jax.ops.segment_sum(msg, dst, num_segments=N)
        deg = jax.ops.segment_sum(jnp.ones((src.shape[0],), dtype=node_feats.dtype), dst, num_segments=N)
        agg_mean = agg_sum / jnp.maximum(deg, 1.0)[:, None]
        h = (1.0 + eps[0]) * node_feats + agg_mean
        h = jax.nn.relu(_batchnorm(h @ W1 + b1, gamma1, beta1))
        h = jax.nn.relu(_batchnorm(h @ W2 + b2, gamma2, beta2))
        return h

    def _L1_gnn_ref(pos, edge_index, W1, b1, W2, b2, W3, b3):
        import jax, jax.numpy as jnp
        import numpy as np
        N_NODES = 3125
        N_CHANNELS = 64
        N_EDGES = 37500
        K_CHEB = 6

        def _cheb_norm(edge_index, num_nodes):
            row, col = (edge_index[0], edge_index[1])
            ones = jnp.ones(edge_index.shape[1], dtype=jnp.float32)
            deg = jax.ops.segment_sum(ones, row, num_segments=num_nodes)
            dinv = jnp.where(deg > 0, jax.lax.rsqrt(jnp.where(deg > 0, deg, 1.0)), 0.0)
            norm = -dinv[row] * dinv[col]
            return norm

        def _propagate(x, row, col, norm, num_nodes):
            msgs = norm[:, None] * x[col]
            return jax.ops.segment_sum(msgs, row, num_segments=num_nodes)

        def _cheb_conv(x, W, b, row, col, norm, num_nodes):
            Tx0 = x
            out = Tx0 @ W[0]
            Tx1 = _propagate(Tx0, row, col, norm, num_nodes)
            out = out + Tx1 @ W[1]
            for k in range(2, W.shape[0]):
                Tx2 = 2.0 * _propagate(Tx1, row, col, norm, num_nodes) - Tx0
                out = out + Tx2 @ W[k]
                Tx0, Tx1 = (Tx1, Tx2)
            return out + b
        num_nodes = pos.shape[0]
        row, col = (edge_index[0], edge_index[1])
        norm = _cheb_norm(edge_index, num_nodes)
        residual = pos
        h = jax.nn.relu(_cheb_conv(pos, W1, b1, row, col, norm, num_nodes))
        h = jax.nn.relu(_cheb_conv(h, W2, b2, row, col, norm, num_nodes))
        h = jax.nn.relu(_cheb_conv(h, W3, b3, row, col, norm, num_nodes))
        return h + residual
    edge_index = jnp.stack([src, dst])
    h = jnp.maximum(_layernorm(x, axis=-1), 0.0)
    x = x + _L0_gnn_ref(h, edge_attr_64, src, dst, L0_gnn_eps, L0_gnn_W1, L0_gnn_b1, L0_gnn_gamma1, L0_gnn_beta1, L0_gnn_W2, L0_gnn_b2, L0_gnn_gamma2, L0_gnn_beta2)
    h = jnp.maximum(_layernorm(x, axis=-1), 0.0)
    x = x + _L1_gnn_ref(h, edge_index, L1_gnn_W1, L1_gnn_b1, L1_gnn_W2, L1_gnn_b2, L1_gnn_W3, L1_gnn_b3)
    return x

_drawn_inputs = setup_inputs


def setup_inputs(seed=0):
    import zlib

    import numpy as np

    out = dict(_drawn_inputs(seed))
    spreads = {'L0_gnn_b1': (0.0, 0.8),
     'L0_gnn_gamma1': (1.0, 0.2),
     'L0_gnn_beta1': (0.0, 0.291),
     'L0_gnn_b2': (0.0, 0.8),
     'L0_gnn_gamma2': (1.0, 0.2),
     'L0_gnn_beta2': (0.0, 0.1),
     'L1_gnn_b1': (0.0, 0.1),
     'L1_gnn_b2': (0.0, 0.269),
     'L1_gnn_b3': (0.0, 0.509)}
    factors = {}
    for name, (base, spread) in spreads.items():
        noise = np.random.default_rng([zlib.crc32(name.encode()), seed]).standard_normal(out[name].shape)
        drawn = base * np.exp(spread * noise) if base else spread * noise
        out[name] = jnp.asarray(drawn.astype(out[name].dtype))
    for name, factor in factors.items():
        out[name] = (out[name] * factor).astype(out[name].dtype)
    return out
```

```python
from collections import namedtuple
from contextlib import ExitStack

import concourse.bass as bass
from concourse import mybir

ALU = mybir.AluOpType
ACT = mybir.ActivationFunctionType
AX = mybir.AxisListType
F32 = mybir.dt.float32
F16 = mybir.dt.float16
BF16 = mybir.dt.bfloat16
I32 = mybir.dt.int32
RMAX = bass.bass_isa.ReduceOp.max
ds = bass.ds

P = 128
BANK = 512
T = 125
WN = 5
WT = T // WN
ROW = 32
WROWS = 8
HALF = WROWS * ROW // P
WPAD = WT + 1
GROUPS = ((0, 7), (7, 6), (13, 7), (20, 6))
GCOLS = 7 * HALF
PARTS = ((0, 13), (13, WT - 13))
CE = 36
SE = 4
NSUB = CE // SE
RING = 3
SPLIT = 4
CHUNK = 4
MAGIC = 12582912.0
PAD_NODE = 4000
HSCALE = 1024.0
TOP = 28000.0
EPS = 1e-5


def record(**fields):
    return namedtuple("Record", list(fields))(**fields)


class Chain:

    def __init__(self, engine, sem):
        self.engine, self.sem, self.base, self.n = engine, sem, 0, 0

    def link(self, instruction):
        self.n += 1
        instruction.then_inc(self.sem, 1)
        self.engine.wait_ge(self.sem, self.base + self.n)

    def turn(self, base):
        self.base, self.n = base, 0


def shapes_of(N, E, D, H, K):
    G = N // T
    NW = N // WN
    RPP = -(-(-(-E // ROW) + WROWS) // P)
    NCH = -(-G // CHUNK)
    s = record(
        N=N, E=E, D=D, H=H, K=K, G=G,
        NW=NW,
        NB=NW // T,
        TB=T // WT,
        M=WN * G,
        RPP=RPP, EPP=RPP * ROW,
        NCH=NCH, chunks=[(n * CHUNK, min(CHUNK, G - n * CHUNK)) for n in range(NCH)],
        RAW=3 * D + 2 * D + 1,
        HW=2 * D + 1)
    assert N == G * T and s.NW == s.NB * T and s.M <= P and E >= P * CE
    assert D == 64 and H == P and K == 6 and 3 * K * D <= 3 * BANK
    return s


def place(nc, s, ctx):
    N, G, D, K = s.N, s.G, s.D, s.K
    tensors = {}
    start = (nc.sbuf_base + 63) // 64 * 64
    top = nc.sbuf_usable_end
    size = {F32: 4, I32: 4, F16: 2, BF16: 2}

    def put(at, end, name, rows, cols, dt):
        nbytes = (cols * size[dt] + 31) // 32 * 32
        assert at + nbytes <= end, (name, at + nbytes, end)
        tensors[name] = nc.alloc_sbuf_tensor_at(name, [rows, cols], dt, offset=at)
        return at + nbytes

    def run(at, end, rows):
        for name, r, cols, dt in rows:
            at = put(at, end, name, r, cols, dt)
        return at

    common = run(start, top, [
        ("ident16", P, P, F16), ("identf", P, P, F32), ("ones16", P, P, F16), ("onesf", P, P, F32),
        ("starts", 1, G, I32), ("flag", 1, 2, I32), ("epst", P, 1, F32)])
    digits = run(common, top, [
        ("mT", P, G * HALF * WPAD, F16), ("lT", P, G * HALF * WPAD, F16), ("rel", P, G * CE, F16),
        ("hs", T, G * s.HW, F16), ("iotaR", P, T * GCOLS, F16)])
    n0 = GCOLS
    c_at = run(digits, top, [
        ("om0", P, T * n0, F16), ("om1", P, T * n0, F16), ("ol0", P, T * n0, F16), ("ol1", P, T * n0, F16),
        ("oe0", P, T * SE, BF16), ("oe1", P, T * SE, BF16), ("oe2", P, T * SE, BF16),
        ("fx0", P, 3 * SE * D, F32), ("fx1", P, 3 * SE * D, F32), ("fx2", P, 3 * SE * D, F32),
        ("bt", T, G * T, F16), ("stage", T, s.RAW, F32),
        ("geni", P, 2, I32), ("gen", P, 4, F32), ("genr", P, G, F32), ("zeros", P, 3 * D, F16)])
    assert G * T <= 2 * T * n0
    tensors["osrc"] = nc.alloc_sbuf_tensor_at("osrc", [P, G * T], F16, offset=digits)
    run(c_at, top, [("C", T, G * N, F16)])
    W = WROWS * ROW
    run(digits, top, [
        ("srci", P, s.EPP, I32), ("dsti", P, s.EPP, I32), ("keyf", P, s.EPP, F32),
        ("rowmax", P, s.RPP, F32), ("wfirst", P, s.NW, F32), ("before", P, s.RPP * s.NW, F16),
        ("iota8", P, WROWS, F32), ("rowidx", P, s.NB * WROWS, I32), ("wkey0", P, s.NB, F32),
        ("kw", P, s.NB * W, F32), ("md", P, s.NB * W, F32), ("lod", P, s.NB * W, F32),
        ("m16", P, s.NB * W, F16), ("l16", P, s.NB * W, F16), ("val", P, s.NB * W, F32),
        ("dk", P, G * CE, I32), ("tfirst", P, G, F32), ("relf", P, G * CE, F32), ("vale", P, G * CE, F32),
        ("cnt", P, 2, F32), ("startf", 1, G, F32), ("flagf", 1, 4, F32),
        ("xa", T, G * D, F32), ("xca", T, G * D, F32), ("sqa", T, G * D, F32), ("sta", T, 4 * G, F32)])
    kept = run(common, c_at, [
        ("dinv", T, G, F32), ("growth", T, 1, F32), ("omega", T, 3 * K, F32),
        ("hN", T, G * D, F32), ("Vt", D + 1, 3 * K * D, F32)])
    vecs = run(kept, c_at, [
        ("hc", T, G * D, F32), ("W1t", D, s.H, F32), ("W2t", s.H, D, F32), ("vec", P, 6, F32), ("mv", P, 8, F32),
        ("stats", P, s.NCH * 6, F32), ("ep1", T, 2, F32), ("stc", T, 4 * G, F32), ("tmp", T, s.TB * D, F32)])
    zed = run(vecs, c_at, [("hT", D, N, F32)])
    run(zed, c_at, [("z1", P, N, F32)])
    run(zed, c_at, [("raw0", T, s.TB * s.RAW, F32), ("raw1", T, s.TB * s.RAW, F32)])
    run(vecs, c_at, [("degrow", 1, N, F32)])
    run(vecs, c_at, [("xcc", T, G * D, F32), ("sqc", T, G * D, F32), ("vabs", D, 3 * K * D, F32)])
    run(kept, c_at, [
        ("vs0", T, G * 2 * D, F16), ("vs1", T, G * 2 * D, F16), ("bB", T, G * D, F32), ("hTc", D + 1, N, F32),
        ("tb0", P, CHUNK * T, F32), ("tb1", P, CHUNK * T, F32), ("JJ", P, D, F32),
        ("ua0", T, CHUNK * D, F32), ("ua1", T, CHUNK * D, F32), ("ub", T, CHUNK * D, F32), ("av", T, G, F32), ("gv", T, G, F32),
        ("mxp", T, 2 * s.NCH, F32), ("mx", T, 8, F32), ("sc", T, 8, F32)])
    def dram(name, shape):
        return nc.dram_tensor(name, shape, F32, kind="Internal").ap()

    return record(
        ps=ctx.enter_context(nc.psum_tensor("ps", [P, 8 * BANK], F32)),
        key_dram=dram("key_dram", [P * s.RPP, ROW]), h_dram=dram("h_dram", [T, G * D]),
        raw_dram=dram("raw_dram", [G * T, s.RAW]), res_dram=dram("res_dram", [T, G * D]), **tensors)


def tiles3(ap, inner):
    return ap.rearrange("p (i c) -> p i c", c=inner)


def wide(ap, n):
    return ap.unsqueeze(2).broadcast_to([ap.shape[0], ap.shape[1], n])


def layernorm(nc, dve, chain, s, xs, xc, sq, st, out, variance_ready, std_ready):
    G, D = s.G, s.D
    x3, xc3, sq3 = tiles3(xs[:, :], D), tiles3(xc[:, :], D), tiles3(sq[:, :], D)
    mean, var, rstd = st[:, 0:G], st[:, G:2 * G], st[:, 3 * G:4 * G]
    chain.link(nc.vector.tensor_reduce(mean, x3, AX.X, ALU.add))
    chain.link(nc.vector.tensor_scalar(mean, mean, 1.0 / D, None, ALU.mult))
    chain.link(nc.vector.tensor_tensor(xc3, x3, wide(mean, D), ALU.subtract))
    chain.link(nc.vector.tensor_tensor(sq[:, :], xc[:, :], xc[:, :], ALU.mult))
    nc.vector.tensor_reduce(var, sq3, AX.X, ALU.add).then_inc(variance_ready, 1)
    dve.wait_ge(std_ready, 1)
    chain.link(nc.vector.reciprocal(rstd, st[:, 2 * G:3 * G]))
    chain.link(nc.vector.tensor_tensor(xc3, xc3, wide(rstd, D), ALU.mult))
    chain.link(nc.vector.tensor_scalar(out[:, :], xc[:, :], 0.0, None, ALU.max))


def layernorm_root(nc, act, s, b, st, variance_ready, std_ready):
    G = s.G
    act.wait_ge(variance_ready, 1)
    nc.scalar.activation(st[:, 2 * G:3 * G], st[:, G:2 * G], ACT.Sqrt, bias=b.epst[0:T, :],
                         scale=1.0 / s.D).then_inc(std_ready, 1)


def keys_phase(nc, s, b, A, sem):
    N, G, D, E, NB, NW, RPP, EPP = s.N, s.G, s.D, s.E, s.NB, s.NW, s.RPP, s.EPP
    W = WROWS * ROW
    full, rest = E // EPP, E % EPP
    pads_set, edges_in, x_in = sem("pads_set"), sem("edges_in"), sem("x_in")
    key_made, key_stored, starts_made = sem("key_made"), sem("key_stored"), sem("starts_made")
    targets_in, h_made, h_stored = sem("targets_in"), sem("h_made"), sem("h_stored")
    iotas_made, rows_made, gathered = sem("iotas_made"), sem("rows_made"), sem("gathered")
    ones_made, ident_made = sem("ones_made"), sem("ident_made")
    before_made, row0_summed, digits_made = sem("before_made"), sem("row0_summed"), sem("digits_made")
    turned, counted, count_summed = sem("turned"), sem("counted"), sem("count_summed")
    var_a, std_a = sem("var_a"), sem("std_a")
    dve_own, pool_own = sem("dve_own_a"), sem("pool_own_a")
    ps = b.ps

    with nc.Block() as block:
        @block.sync
        def _(sp):
            sp.dma_start(tiles3(b.xa[:, :], D), A.x.rearrange("(i p) c -> p i c", p=T)).then_inc(x_in, 16)
            sp.wait_ge(pads_set, 2)
            loads = 0
            for edge, tile in ((A.dst, b.dsti), (A.src, b.srci)):
                if full:
                    sp.dma_start(tile[0:full, :], edge[0:full * EPP].rearrange("(p c) -> p c", c=EPP)).then_inc(
                        edges_in, 16)
                if rest:
                    sp.dma_start(tile[full:full + 1, 0:rest],
                                 edge[full * EPP:E].rearrange("(p c) -> p c", p=1)).then_inc(edges_in, 16)
            sp.wait_ge(key_made, 1)
            sp.dma_start(b.key_dram.rearrange("(p r) c -> p (r c)", p=P), b.keyf[:, :]).then_inc(key_stored, 16)
            sp.wait_ge(h_made, 1)
            sp.dma_start(b.h_dram, b.xca[:, :]).then_inc(h_stored, 16)
            sp.wait_ge(starts_made, 1)
            with sp.Fori(0, G) as i:
                first = sp.value_load(b.starts[0:1, ds(i, 1)], min_val=0, max_val=E - P * CE)
                sp.dma_start(b.dk[:, ds(i * CE, CE)],
                             A.dst[ds(first, P * CE)].rearrange("(p c) -> p c", p=P)).then_inc(targets_in, 16)
            sp.wait_ge(targets_in, 16 * G)
            sp.wait_ge(h_stored, 16)
            sp.wait_ge(key_stored, 16)

        @block.gpsimd
        def _(pool):
            chain = Chain(pool, pool_own)
            nc.gpsimd.memset(b.srci[:, :], 0).then_inc(pads_set, 1)
            nc.gpsimd.memset(b.dsti[:, :], PAD_NODE).then_inc(pads_set, 1)
            nc.gpsimd.memset(b.ones16[:, :], 1.0).then_inc(ones_made, 1)
            nc.gpsimd.memset(b.onesf[:, :], 1.0).then_inc(ones_made, 1)
            io = dict(allow_small_or_imprecise_dtypes=True)
            nc.gpsimd.iota(b.wfirst[:, :], [[WN, NW]], base=0, channel_multiplier=0, **io).then_inc(iotas_made, 1)
            nc.gpsimd.iota(b.iota8[:, :], [[1, WROWS]], base=0, channel_multiplier=0, **io).then_inc(iotas_made, 1)
            nc.gpsimd.iota(b.tfirst[:, :], [[T, G]], base=0, channel_multiplier=0, **io).then_inc(iotas_made, 1)
            nc.gpsimd.iota(b.wkey0[:, :], [[T, NB]], base=0, channel_multiplier=1, **io).then_inc(iotas_made, 1)
            nc.gpsimd.iota(b.iotaR[:, :], [[1, T], [0, GCOLS]], base=0, channel_multiplier=0,
                           **io).then_inc(iotas_made, 1)
            nc.gpsimd.memset(b.epst[:, :], EPS).then_inc(ident_made, 1)
            chain.link(nc.gpsimd.memset(b.ident16[:, :], 0.0))
            chain.link(nc.gpsimd.memset(b.identf[:, :], 0.0))
            for t in (b.ident16, b.identf):
                nc.gpsimd.affine_select(out=t[:, :], in_=t[:, :], compare_op=ALU.not_equal, fill=1.0, base=0,
                                        pattern=[[-1, P]], channel_multiplier=1).then_inc(ident_made, 1)
            nc.gpsimd.memset(b.mT[:, :], -1.0).then_inc(ident_made, 1)
            nc.gpsimd.memset(b.lT[:, :], -1.0).then_inc(ident_made, 1)
            nc.gpsimd.memset(tiles3(b.hs[:, :], s.HW)[:, :, 2 * D:], 1.0).then_inc(ident_made, 1)
            nc.gpsimd.memset(b.cnt[:, :], 0.0).then_inc(ident_made, 1)
            nc.gpsimd.memset(b.flagf[:, :], 0.0).then_inc(ident_made, 1)
            pool.wait_ge(key_stored, 16)
            pool.wait_ge(rows_made, NB)
            for j in range(NB):
                for k in range(WROWS):
                    n = j * WROWS + k
                    nc.gpsimd.indirect_dma_start(
                        b.kw[0:T, n * ROW:(n + 1) * ROW], None, b.key_dram,
                        bass.IndirectOffsetOnAxis(ap=b.rowidx[0:T, n:n + 1], axis=0)).then_inc(gathered, 16)
            pool.wait_ge(gathered, 16 * NB * WROWS)

        @block.tensor
        def _(pe):
            pe.wait_ge(ones_made, 2)
            pe.wait_ge(before_made, RPP)
            for j in range(NB):
                for r in range(RPP):
                    at = r * NW + j * T
                    nc.tensor.matmul(ps[0:T, j:j + 1], b.before[:, at:at + T], b.ones16[:, 0:1],
                                     start=(r == 0), stop=(r == RPP - 1))
            windows = tiles3(b.before[:, :], WT)
            for r in range(RPP):
                last = nc.tensor.matmul(ps[0:1, BANK:BANK + G], b.ones16[:, 0:1],
                                        windows[:, r * G:(r + 1) * G, 0], start=(r == 0), stop=(r == RPP - 1))
            last.then_inc(row0_summed, 1)
            pe.wait_ge(digits_made, 2)
            pe.wait_ge(ident_made, 3)
            for t, digit in enumerate((b.m16, b.l16)):
                for q in range(NB * HALF):
                    at = (2 + 3 * t) * BANK + q * P
                    last = nc.tensor.matmul(ps[:, at:at + T], digit[0:T, q * P:(q + 1) * P],
                                            b.ident16[0:T, 0:T], start=True, stop=True)
                last.then_inc(turned, 1)
            pe.wait_ge(counted, 2)
            nc.tensor.matmul(ps[0:1, 0:2], b.onesf[:, 0:1], b.cnt[:, :], start=True,
                             stop=True).then_inc(count_summed, 1)

        @block.scalar
        def _(act):
            act.wait_ge(ident_made, 1)
            layernorm_root(nc, act, s, b, b.sta, var_a, std_a)

        @block.vector
        def _(dve):
            chain = Chain(dve, dve_own)
            link = chain.link
            dve.wait_ge(edges_in, 16 * 2 * (bool(full) + bool(rest)))
            nc.vector.scalar_tensor_tensor(b.keyf[:, :], b.dsti[:, :], float(N), b.srci[:, :], ALU.mult,
                                           ALU.add).then_inc(key_made, 1)
            link(nc.vector.tensor_reduce(b.rowmax[:, :], tiles3(b.dsti[:, :], ROW), AX.X, ALU.max))
            dve.wait_ge(iotas_made, 5)
            for r in range(RPP):
                nc.vector.tensor_scalar(b.before[:, r * NW:(r + 1) * NW], b.wfirst[:, :], b.rowmax[:, r:r + 1],
                                        None, ALU.is_gt).then_inc(before_made, 1)
            dve.wait_ge(row0_summed, 1)
            for j in range(NB):
                nc.vector.tensor_scalar(b.rowidx[0:T, j * WROWS:(j + 1) * WROWS], b.iota8[0:T, :],
                                        ps[0:T, j:j + 1], None, ALU.add).then_inc(rows_made, 1)
            nc.vector.tensor_scalar(b.starts[0:1, :], ps[0:1, BANK:BANK + G], float(ROW), float(E - P * CE),
                                    ALU.mult, ALU.min).then_inc(starts_made, 1)
            dve.wait_ge(x_in, 16)
            layernorm(nc, dve, chain, s, b.xa, b.xca, b.sqa, b.sta, b.xca, var_a, std_a)
            dve.sem_inc(h_made, 1)
            hs3 = tiles3(b.hs[:, :], s.HW)
            dve.wait_ge(ident_made, 8)
            link(nc.vector.tensor_scalar(b.sqa[:, :], b.xca[:, :], HSCALE, None, ALU.mult))
            sq3 = tiles3(b.sqa[:, :], D)
            link(nc.vector.tensor_copy(hs3[:, :, 0:D], sq3))
            link(nc.vector.tensor_tensor(hs3[:, :, D:2 * D], sq3, hs3[:, :, 0:D], ALU.subtract))
            link(nc.vector.tensor_scalar(b.wkey0[:, :], b.wkey0[:, :], float(WN * N), None, ALU.mult))
            dve.wait_ge(gathered, 16 * NB * WROWS)
            for j in range(NB):
                link(nc.vector.tensor_scalar(b.kw[0:T, j * W:(j + 1) * W], b.kw[0:T, j * W:(j + 1) * W],
                                             b.wkey0[0:T, j:j + 1], None, ALU.subtract))
            kw, md, lod, val = b.kw[0:T, :], b.md[0:T, :], b.lod[0:T, :], b.val[0:T, :]
            link(nc.vector.tensor_scalar(md, kw, 1.0 / T, -(T // 2) / T, ALU.mult, ALU.add))
            link(nc.vector.tensor_scalar(md, md, MAGIC, None, ALU.add))
            link(nc.vector.tensor_scalar(md, md, MAGIC, None, ALU.subtract))
            link(nc.vector.scalar_tensor_tensor(lod, md, -float(T), kw, ALU.mult, ALU.add))
            nc.vector.tensor_scalar(b.l16[0:T, :], lod, -1.0, float(P), ALU.max, ALU.min).then_inc(digits_made, 1)
            nc.vector.tensor_scalar(b.m16[0:T, :], md, -1.0, float(P), ALU.max, ALU.min).then_inc(digits_made, 1)
            link(nc.vector.tensor_scalar(val, md, s.M - 0.5, None, ALU.is_le))
            nc.vector.scalar_tensor_tensor(kw, md, -0.5, val, ALU.is_ge, ALU.mult,
                                           accum_out=b.cnt[0:T, 0:1]).then_inc(counted, 1)
            dve.wait_ge(targets_in, 16 * G)
            link(nc.vector.tensor_tensor(tiles3(b.relf[:, :], CE), tiles3(b.dk[:, :], CE), wide(b.tfirst[:, :], CE),
                                         ALU.subtract))
            link(nc.vector.tensor_scalar(b.vale[:, :], b.relf[:, :], T - 0.5, None, ALU.is_le))
            link(nc.vector.tensor_scalar(b.rel[:, :], b.relf[:, :], -1.0, float(P), ALU.max, ALU.min))
            nc.vector.scalar_tensor_tensor(b.relf[:, :], b.relf[:, :], -0.5, b.vale[:, :], ALU.is_ge, ALU.mult,
                                           accum_out=b.cnt[:, 1:2]).then_inc(counted, 1)
            for t, turn in enumerate((b.mT, b.lT)):
                dve.wait_ge(turned, t + 1)
                view = turn[:, :].rearrange("p (i w h) -> p i w h", h=HALF, w=WPAD)
                for j in range(NB):
                    for h in range(HALF):
                        at = (2 + 3 * t) * BANK + (j * HALF + h) * P
                        link(nc.vector.tensor_copy(view[:, j * s.TB:(j + 1) * s.TB, 0:WT, h],
                                                   tiles3(ps[:, at:at + T], WT)))
            dve.wait_ge(count_summed, 1)
            link(nc.vector.tensor_scalar(b.flagf[:, 0:2], ps[0:1, 0:2], float(E), None, ALU.is_equal))
            link(nc.vector.tensor_tensor(b.flag[:, 0:1], b.flagf[:, 0:1], b.flagf[:, 1:2], ALU.mult))


def finish_tile(nc, s, b, pe, i, q):
    G, D = s.G, s.D
    pe.wait_ge(q.bt_made, 2 * i + 3)
    for k in range(G):
        last = nc.tensor.matmul(b.ps[0:T, 7 * BANK + 3 * D:7 * BANK + s.RAW], b.bt[:, k * T:(k + 1) * T],
                                b.hs[:, k * s.HW:(k + 1) * s.HW], start=(k == 0), stop=(k == G - 1))
    last.then_inc(q.sums_made, 1)
    for n, (k0, kn) in enumerate(s.chunks):
        before = n - 3 if n >= 3 else max(c for c in range(s.NCH) if c % 3 == n) - s.NCH
        pe.wait_ge(q.c_stored, i * s.NCH + (before + 1 + 3))
        for k in range(k0, k0 + kn):
            at = (4 + n % 3) * BANK + (k - k0) * T
            last = nc.tensor.matmul(b.ps[0:T, at:at + T], b.bt[:, k * T:(k + 1) * T], b.ident16[0:T, 0:T],
                                    start=True, stop=True)
        last.then_inc(q.c_turned, 1)


def start_counts(act, q):
    act.sem_inc(q.c_stored, 3)
    act.sem_inc(q.bt_made, 1)
    act.sem_inc(q.staged, 1)
    act.sem_inc(q.c_turned, 1)
    act.sem_inc(q.raw_stored, 16)


def store_tile(nc, s, b, act, i, q, C3):
    act.wait_ge(q.sums_made, i + 1)
    act.wait_ge(q.raw_stored, 16 * i + 16)
    nc.scalar.activation(b.stage[:, :], b.ps[0:T, 7 * BANK:7 * BANK + s.RAW], ACT.Copy).then_inc(q.staged, 1)
    for n, (k0, kn) in enumerate(s.chunks):
        act.wait_ge(q.c_turned, i * s.NCH + n + 2)
        at = (4 + n % 3) * BANK
        nc.scalar.activation(b.C[:, ds(i * s.N + k0 * T, kn * T)], b.ps[0:T, at:at + kn * T],
                             ACT.Copy).then_inc(q.c_stored, 1)
    act.wait_ge(q.staged, i + 2)
    act.dma_start(b.raw_dram[ds(i * T, T), :], b.stage[:, :]).then_inc(q.raw_stored, 16)


def feature_parts(nc, pool, chain, fx, n):
    fx3 = fx[:, :].rearrange("p (t c) -> p t c", t=3)
    hi = fx[:, :].bitcast(BF16).rearrange("p (t c two) -> p t c two", t=3, two=2)
    chain.link(nc.gpsimd.tensor_tensor(fx3[:, 1, 0:n], fx3[:, 0, 0:n], hi[:, 0, 0:n, 1], ALU.subtract))
    return nc.gpsimd.tensor_tensor(fx3[:, 2, 0:n], fx3[:, 1, 0:n], hi[:, 1, 0:n, 1], ALU.subtract)


def feature_view(fx, slot_edges, e, D):
    return fx[:, :].bitcast(BF16).rearrange("p (t j c two) -> p t j c two", t=3, j=slot_edges, two=2)[:, :, e, :, 1]


def counts_sems(sem, tag):
    names = ("groups_made", "groups_used", "zeros_set", "waited", "bt_made", "sums_made", "c_turned", "c_stored", "staged",
             "raw_stored", "feats_in0", "feats_in1", "feats_in2", "feats_split", "hots_made", "sub_used", "act_own", "dve_own", "pool_own")
    return record(**{n: sem(n + tag) for n in names})


def sorted_counts(nc, s, b, A, q):
    N, G, D, E, M = s.N, s.G, s.D, s.E, s.M
    fx, oe = (b.fx0, b.fx1, b.fx2), (b.oe0, b.oe1, b.oe2)
    om, ol = (b.om0, b.om1), (b.ol0, b.ol1)
    feats_in = (q.feats_in0, q.feats_in1, q.feats_in2)

    def sync(sp):
        with sp.Fori(0, G) as i:
            first = sp.value_load(b.starts[0:1, ds(i, 1)], min_val=0, max_val=E - P * CE)
            feats = A.edge_attr[ds(first, P * CE), :].rearrange("(p c) d -> p c d", p=P)
            for k in range(NSUB):
                sp.wait_ge(q.sub_used, i * NSUB + k + 1)
                sp.dma_start(fx[k % RING][:, 0:SE * D].rearrange("p (c d) -> p c d", d=D),
                             feats[:, k * SE:(k + 1) * SE, :]).then_inc(feats_in[k % RING], 16)

    def gpsimd(pool):
        chain = Chain(pool, q.pool_own)
        with pool.Fori(0, G) as i:
            chain.turn(i * NSUB)
            for k in range(NSUB):
                pool.wait_ge(feats_in[k % RING], 16 * (i * (NSUB // RING) + k // RING + 1))
                feature_parts(nc, pool, chain, fx[k % RING], SE * D).then_inc(q.feats_split, 1)

    def vector(dve):
        iota3 = tiles3(b.iotaR[:, :], GCOLS)

        def group(i, g):
            w0, wn = GROUPS[g][0], GROUPS[g][1] * HALF
            at = i * (HALF * WPAD) + w0 * HALF
            dve.wait_ge(q.groups_used, i * 4 + g + 1)
            for digit, hot, rows in ((b.mT, om, M), (b.lT, ol, T)):
                last = nc.vector.tensor_tensor(
                    tiles3(hot[g % 2][:, 0:rows * wn], wn),
                    digit[:, ds(at, wn)].unsqueeze(1).broadcast_to([P, rows, wn]),
                    iota3[:, 0:rows, 0:wn], ALU.is_equal)
            last.then_inc(q.groups_made, 1)

        def sub(i, k):
            dve.wait_ge(q.sub_used, i * NSUB + k + 1)
            nc.vector.tensor_tensor(
                tiles3(oe[k % RING][:, :], SE),
                b.rel[:, ds(i * CE + k * SE, SE)].unsqueeze(1).broadcast_to([P, T, SE]),
                iota3[:, 0:T, 0:SE], ALU.is_equal).then_inc(q.hots_made, 1)

        with dve.Fori(0, G) as i:
            group(i, 0)
            group(i, 1)
            for k in range(SPLIT):
                sub(i, k)
            group(i, 2)
            group(i, 3)
            for k in range(SPLIT, NSUB):
                sub(i, k)

    def tensor(pe):
        pe.sem_inc(q.groups_used, 2)
        pe.sem_inc(q.sub_used, RING)

        def part(i, p):
            if p:
                pe.wait_ge(q.bt_made, i * 2 + 2)
            else:
                pe.wait_ge(q.bt_made, i * 2 + 1)
            for g in (2 * p, 2 * p + 1):
                pe.wait_ge(q.groups_made, i * 4 + g + 1)
                w0, wn = GROUPS[g]
                cols = wn * HALF
                o_m, o_l = tiles3(om[g % 2][:, 0:M * cols], cols), tiles3(ol[g % 2][:, 0:T * cols], cols)
                for w in range(min(wn, WT - w0)):
                    at = (w0 - PARTS[p][0] + w) * P
                    for h in range(HALF):
                        last = nc.tensor.matmul(b.ps[0:T, at:at + M], o_l[:, :, w * HALF + h],
                                                o_m[:, :, w * HALF + h], start=(h == 0), stop=(h == HALF - 1))
                last.then_inc(q.groups_used, 1)

        def sub(i, k):
            if k == 0:
                pe.wait_ge(q.staged, i + 1)
            pe.wait_ge(q.hots_made, i * NSUB + k + 1)
            pe.wait_ge(q.feats_split, i * NSUB + k + 1)
            hot = tiles3(oe[k % RING][:, :], SE)
            for e in range(SE):
                n = k * SE + e
                last = nc.tensor.matmul(
                    b.ps[0:T, 7 * BANK:7 * BANK + 3 * D].rearrange("p (t c) -> p t c", t=3), hot[:, :, e],
                    feature_view(fx[k % RING], SE, e, D), start=(n == 0), stop=(n == CE - 1))
            last.then_inc(q.sub_used, 1)

        with pe.Fori(0, G) as i:
            part(i, 0)
            for k in range(SPLIT):
                sub(i, k)
            part(i, 1)
            for k in range(SPLIT, NSUB):
                sub(i, k)
            finish_tile(nc, s, b, pe, i, q)

    def scalar(act):
        start_counts(act, q)
        with act.Fori(0, G) as i:
            act.wait_ge(q.c_turned, i * s.NCH + 1)
            for p in range(2):
                act.wait_ge(q.groups_used, 2 + i * 4 + 2 * p + 2)
                w0, real = PARTS[p]
                counts = b.ps[0:T, 0:real * P].rearrange("p (w m) -> p w m", m=P)[:, :, 0:M]
                counts = counts.rearrange("p w (d k) -> p w d k", k=G)
                to = b.bt[:, :].rearrange("p (k w d) -> p w d k", d=WN, w=WT)[:, w0:w0 + real]
                nc.scalar.activation(to, counts, ACT.Copy).then_inc(q.bt_made, 1)
            store_tile(nc, s, b, act, i, q, None)
        act.wait_ge(q.raw_stored, 16 * G + 16)

    return record(sync=sync, gpsimd=gpsimd, vector=vector, tensor=tensor, scalar=scalar)


def counts_phase(nc, s, b, A, sem):
    fast = sorted_counts(nc, s, b, A, counts_sems(sem, "_sorted"))
    slow = general_counts(nc, s, b, A, counts_sems(sem, "_any"))

    def either(engine, one, other):
        covered = engine.value_load(b.flag[0:1, 0:1], min_val=0, max_val=1)
        with engine.If(covered == 1):
            one(engine)
        with engine.Else():
            other(engine)

    with nc.Block() as block:
        @block.sync
        def _(sp):
            either(sp, fast.sync, slow.sync)

        @block.gpsimd
        def _(pool):
            either(pool, fast.gpsimd, slow.gpsimd)

        @block.vector
        def _(dve):
            either(dve, fast.vector, slow.vector)

        @block.tensor
        def _(pe):
            either(pe, fast.tensor, slow.tensor)

        @block.scalar
        def _(act):
            either(act, fast.scalar, slow.scalar)


def general_counts(nc, s, b, A, q):
    N, G, D, E = s.N, s.G, s.D, s.E
    full, rest = E // P, E % P
    turns = full + bool(rest)

    def steps(engine, step):
        with engine.Fori(0, G) as i:
            step.before(i)
            with engine.Fori(0, full) as j:
                step(i, i * turns + j, j * P, P)
            if rest:
                step(i, i * turns + full, full * P, rest)
            step.after(i)

    class Step:
        def __init__(self, body, before=lambda i: None, after=lambda i: None):
            self.body, self.before, self.after = body, before, after

        def __call__(self, *a):
            self.body(*a)

    def sync(sp):
        def load(i, n, at, rows):
            sp.wait_ge(q.sub_used, n + 1)
            sp.dma_start(b.geni[0:rows, 0:1], A.src[ds(at, rows)].unsqueeze(1)).then_inc(q.feats_in0, 16)
            sp.dma_start(b.geni[0:rows, 1:2], A.dst[ds(at, rows)].unsqueeze(1)).then_inc(q.feats_in0, 16)
            sp.dma_start(b.fx0[0:rows, 0:D], A.edge_attr[ds(at, rows), :]).then_inc(q.feats_in0, 16)
        steps(sp, Step(load))

    def gpsimd(pool):
        chain = Chain(pool, q.pool_own)

        chain.link(nc.gpsimd.memset(b.fx0[:, :], 0.0))
        chain.link(nc.gpsimd.memset(b.zeros[:, :], 0.0))
        pool.sem_inc(q.zeros_set, 1)
        pool.sem_inc(q.sub_used, 1)

        def split(i, n, at, rows):
            chain.turn(n + 2)
            pool.wait_ge(q.feats_in0, 48 * (n + 1))
            feature_parts(nc, pool, chain, b.fx0, D).then_inc(q.feats_split, 1)
        steps(pool, Step(split))

    def vector(dve):
        chain = Chain(dve, q.dve_own)
        first, iota = b.gen[:, 2:3], tiles3(b.iotaR[:, :], GCOLS)[:, :, 0]
        chain.link(nc.vector.memset(b.gen[:, :], 0.0))
        chain.link(nc.vector.memset(b.oe0[:, :], 0.0))
        chain.link(nc.vector.memset(b.osrc[:, :], 0.0))
        for k in range(G):
            chain.link(nc.vector.memset(b.genr[:, k:k + 1], float(k * T)))
        per = 4

        def hots(i, n, at, rows):
            chain.turn(G + 3 + i + n * per)
            dve.wait_ge(q.feats_in0, 48 * (n + 1))
            chain.link(nc.vector.tensor_copy(b.gen[0:rows, 0:2], b.geni[0:rows, :]))
            chain.link(nc.vector.tensor_tensor(b.gen[0:rows, 3:4], b.gen[0:rows, 1:2], first[0:rows], ALU.subtract))
            chain.link(nc.vector.tensor_scalar(b.oe1[0:rows, 0:T], iota[0:rows], b.gen[0:rows, 3:4], None, ALU.is_equal))
            for k in range(G):
                last = nc.vector.tensor_scalar(b.osrc[0:rows, k * T:(k + 1) * T], iota[0:rows],
                                               b.genr[0:rows, k:k + 1], b.gen[0:rows, 0:1], ALU.add, ALU.is_equal)
            chain.link(last)
            dve.sem_inc(q.hots_made, 1)
            dve.wait_ge(q.sub_used, n + 2)
            dve.sem_inc(q.waited, 1)

        def next_tile(i):
            chain.turn(G + 3 + i + (i + 1) * turns * per)
            chain.link(nc.vector.tensor_scalar(first, first, float(T), None, ALU.add))
        steps(dve, Step(hots, after=next_tile))

    def tensor(pe):
        features = b.ps[0:T, 7 * BANK:7 * BANK + 3 * D]

        def all_zero(first):
            for k in range(G):
                nc.tensor.matmul(b.ps[0:T, k * P:k * P + T], b.zeros[:, 0:T], b.zeros[:, 0:T],
                                 start=first, stop=not first, skip_group_check=True)
            return nc.tensor.matmul(features, b.zeros[:, 0:T], b.zeros[:, :], start=first, stop=not first,
                                    skip_group_check=True)

        def open_tile(i):
            pe.wait_ge(q.zeros_set, 1)
            pe.wait_ge(q.staged, i + 1)
            pe.wait_ge(q.c_stored, i * s.NCH + 3)
            all_zero(True)

        def add(i, n, at, rows):
            pe.wait_ge(q.hots_made, n + 1)
            pe.wait_ge(q.feats_split, n + 1)
            for k in range(G):
                nc.tensor.matmul(b.ps[0:T, k * P:k * P + T], b.osrc[0:rows, k * T:(k + 1) * T], b.oe1[0:rows, 0:T],
                                 start=False, stop=False, skip_group_check=True)
            nc.tensor.matmul(features.rearrange("p (t c) -> p t c", t=3), b.oe1[0:rows, 0:T],
                             feature_view(b.fx0, SE, 0, D)[0:rows], start=False, stop=False,
                             skip_group_check=True).then_inc(q.sub_used, 1)

        def close_tile(i):
            all_zero(False).then_inc(q.groups_used, 1)
            finish_tile(nc, s, b, pe, i, q)
        steps(pe, Step(add, before=open_tile, after=close_tile))

    def scalar(act):
        start_counts(act, q)
        with act.Fori(0, G) as i:
            act.wait_ge(q.groups_used, i + 1)
            counts = b.ps[0:T, 0:G * P].rearrange("p (k m) -> p k m", m=P)[:, :, 0:T]
            nc.scalar.activation(tiles3(b.bt[:, :], T), counts, ACT.Copy).then_inc(q.bt_made, 2)
            store_tile(nc, s, b, act, i, q, None)
        act.wait_ge(q.raw_stored, 16 * G + 16)

    return record(sync=sync, gpsimd=gpsimd, vector=vector, tensor=tensor, scalar=scalar)


def batchnorm_dve(nc, dve, link, b, rows, vec0, var_ready, std_ready, coeffs_ready):
    mv, vec, at = b.mv[0:rows, :], b.vec[0:rows, :], vec0
    nc.vector.bn_aggr(mv[:, 0:2], b.stats[0:rows, :]).then_inc(var_ready, 1)
    dve.wait_ge(std_ready, 1)
    link(nc.vector.reciprocal(mv[:, 3:4], mv[:, 2:3]))
    link(nc.vector.tensor_tensor(mv[:, 4:5], mv[:, 3:4], vec[:, at + 1:at + 2], ALU.mult))
    link(nc.vector.tensor_tensor(mv[:, 5:6], mv[:, 0:1], mv[:, 4:5], ALU.mult))
    nc.vector.tensor_tensor(mv[:, 6:7], vec[:, at + 2:at + 3], mv[:, 5:6], ALU.subtract).then_inc(coeffs_ready, 1)


def perceptron_phase(nc, s, b, A, sem):
    N, G, D, H, K, NCH, RAW, TB = s.N, s.G, s.D, s.H, s.K, s.NCH, s.RAW, s.TB
    ps = b.ps
    weights_in, h_in, raw_in, x_in = sem("weights_in"), sem("h_in"), (sem("raw_in0"), sem("raw_in1")), sem("x_in_c")
    raw_used, hcat_made, rows_set = sem("raw_used"), sem("hcat_made"), sem("rows_set")
    deg_summed, deg_copied, deg_turned, deg_safe, deg_root = (
        sem("deg_summed"), sem("deg_copied"), sem("deg_turned"), sem("deg_safe"), sem("deg_root"))
    eps_wide, deg_max, deg_allmax, growth_made = sem("eps_wide"), sem("deg_max"), sem("deg_allmax"), sem("growth_made")
    h_turned, h_copied, z1_made, z1_copied = sem("h_turned"), sem("h_copied"), sem("z1_made"), sem("z1_copied")
    var_1, std_1, bn1_made, a1_made = sem("var_1"), sem("std_1"), sem("bn1_made"), sem("a1_made")
    z2_made, z2_copied, z2_seen = sem("z2_made"), sem("z2_copied"), sem("z2_seen")
    var_2, std_2, bn2_made, a2_made = sem("var_2"), sem("std_2"), sem("bn2_made"), sem("a2_made")
    a2_turned, a2_used, var_c, std_c = sem("a2_turned"), sem("a2_used"), sem("var_c"), sem("std_c")
    abs_made, omega_summed, res_made, res_stored = sem("abs_made"), sem("omega_summed"), sem("res_made"), sem("res_stored")
    dve_own, eps_used = sem("dve_own_c"), sem("eps_used")
    raw = (b.raw0, b.raw1)
    V = ((A.V1, A.c1), (A.V2, A.c2), (A.V3, A.c3))
    vectors = ((A.b1, H), (A.gamma1, H), (A.beta1, H), (A.b2, D), (A.gamma2, D), (A.beta2, D))
    n_weights = 3 + len(vectors) + 3 * (K + 1)

    def col(v):
        return v.unsqueeze(1)

    with nc.Block() as block:
        @block.sync
        def _(sp):
            sp.dma_start(b.hc[:, :], b.h_dram).then_inc(h_in, 16)
            for j in range(s.NB):
                if j >= 2:
                    sp.wait_ge(raw_used, j - 1)
                sp.dma_start(raw[j % 2][:, :].rearrange("p (u c) -> p u c", c=RAW),
                             b.raw_dram[j * TB * T:(j + 1) * TB * T, :].rearrange("(u p) c -> p u c", p=T)
                             ).then_inc(raw_in[j % 2], 16)
            sp.wait_ge(h_turned, NCH)
            sp.dma_start(tiles3(b.hc[:, :], D), A.x.rearrange("(i p) c -> p i c", p=T)).then_inc(x_in, 16)
            sp.wait_ge(res_made, 1)
            sp.dma_start(b.res_dram, b.hc[:, :]).then_inc(res_stored, 16)
            sp.wait_ge(res_stored, 16)

        @block.gpsimd
        def _(pool):
            nc.gpsimd.memset(b.Vt[D:D + 1, :], 0.0).then_inc(rows_set, 1)
            pool.dma_start(b.W1t[:, :], A.W1).then_inc(weights_in, 16)
            pool.dma_start(b.W2t[:, :], A.W2).then_inc(weights_in, 16)
            pool.dma_start(b.ep1[0:1, 0:1], A.eps.unsqueeze(1)).then_inc(weights_in, 16)
            for n, (v, rows) in enumerate(vectors):
                pool.dma_start(b.vec[0:rows, n:n + 1], col(v)).then_inc(weights_in, 16)
            pool.wait_ge(rows_set, 1)
            for layer, (w, c) in enumerate(V):
                at = layer * K * D
                for r in range(K):
                    pool.dma_start(b.Vt[0:D, at + r * D:at + (r + 1) * D], w[K - 1 - r, :, :]).then_inc(weights_in, 16)
                pool.dma_start(b.Vt[D:D + 1, at + (K - 1) * D:at + K * D], c.unsqueeze(0)).then_inc(weights_in, 16)
            pool.wait_ge(weights_in, 16 * n_weights)
            pool.wait_ge(deg_max, 1)
            nc.gpsimd.partition_all_reduce(b.growth[:, :], b.growth[:, :], T,
                                           RMAX).then_inc(deg_allmax, 1)

        @block.tensor
        def _(pe):
            pe.wait_ge(weights_in, 16 * n_weights)
            nc.tensor.matmul(ps[0:T, 7 * BANK + G:7 * BANK + G + 1], b.onesf[0:1, 0:T], b.ep1[0:1, 0:1], start=True,
                             stop=True).then_inc(eps_wide, 1)
            for n, (k0, kn) in enumerate(s.chunks):
                for k in range(G):
                    last = nc.tensor.matmul(ps[0:1, n * BANK:n * BANK + kn * T], b.ones16[0:T, 0:1],
                                            b.C[:, k * N + k0 * T:k * N + (k0 + kn) * T], start=(k == 0),
                                            stop=(k == G - 1))
                last.then_inc(deg_summed, 1)
            pe.wait_ge(deg_copied, NCH)
            pe.wait_ge(eps_used, 1)
            for k in range(G):
                last = nc.tensor.matmul(ps[0:T, 7 * BANK + k:7 * BANK + k + 1], b.degrow[0:1, k * T:(k + 1) * T],
                                        b.onesf[0:1, 0:1], start=True, stop=True)
            last.then_inc(deg_turned, 1)
            pe.wait_ge(hcat_made, 1)
            for n, (k0, kn) in enumerate(s.chunks):
                if n >= 2:
                    pe.wait_ge(h_copied, n - 1)
                for k in range(kn):
                    at = (n % 2) * BANK + k * T
                    last = nc.tensor.matmul(ps[0:D, at:at + T], b.hc[:, (k0 + k) * D:(k0 + k + 1) * D],
                                            b.identf[0:T, 0:T], start=True, stop=True)
                last.then_inc(h_turned, 1)
            for n, (k0, kn) in enumerate(s.chunks):
                pe.wait_ge(h_copied, n + 1)
                if n >= 2:
                    pe.wait_ge(z1_copied, n - 1)
                nc.tensor.matmul(ps[:, (2 + n % 2) * BANK:(2 + n % 2) * BANK + kn * T], b.W1t[:, :],
                                 b.hT[:, k0 * T:(k0 + kn) * T], start=True, stop=True).then_inc(z1_made, 1)
            for n, (k0, kn) in enumerate(s.chunks):
                pe.wait_ge(a1_made, n + 1)
                if n >= 2:
                    pe.wait_ge(z2_copied, n - 1)
                nc.tensor.matmul(ps[0:D, (4 + n % 2) * BANK:(4 + n % 2) * BANK + kn * T], b.W2t[:, :],
                                 b.z1[:, k0 * T:(k0 + kn) * T], start=True, stop=True).then_inc(z2_made, 1)
            for n, (k0, kn) in enumerate(s.chunks):
                pe.wait_ge(a2_made, n + 1)
                if n >= 2:
                    pe.wait_ge(a2_used, n - 1)
                for k in range(kn):
                    at = (n % 2) * BANK + k * D
                    last = nc.tensor.matmul(ps[0:T, at:at + D], b.hT[:, (k0 + k) * T:(k0 + k + 1) * T],
                                            b.identf[0:D, 0:D], start=True, stop=True)
                last.then_inc(a2_turned, 1)
            pe.wait_ge(abs_made, 1)
            for layer in range(3):
                last = nc.tensor.matmul(ps[0:T, (2 + layer) * BANK:(2 + layer) * BANK + K * D], b.onesf[0:D, 0:T],
                                        b.vabs[:, layer * K * D:(layer + 1) * K * D], start=True, stop=True)
            last.then_inc(omega_summed, 1)

        @block.scalar
        def _(act):
            for n, (k0, kn) in enumerate(s.chunks):
                act.wait_ge(deg_summed, n + 1)
                nc.scalar.activation(b.degrow[0:1, k0 * T:(k0 + kn) * T], ps[0:1, n * BANK:n * BANK + kn * T],
                                     ACT.Copy).then_inc(deg_copied, 1)
            act.wait_ge(deg_safe, 1)
            nc.scalar.activation(b.stc[:, G:2 * G], b.stc[:, 0:G], ACT.Sqrt).then_inc(deg_root, 1)
            act.wait_ge(deg_allmax, 1)
            nc.scalar.activation(b.growth[:, :], b.growth[:, :], ACT.Sqrt, scale=4.0).then_inc(growth_made, 1)
            act.wait_ge(deg_turned, 1)
            for n, (k0, kn) in enumerate(s.chunks):
                act.wait_ge(h_turned, n + 1)
                nc.scalar.activation(b.hT[:, k0 * T:(k0 + kn) * T], ps[0:D, (n % 2) * BANK:(n % 2) * BANK + kn * T],
                                     ACT.Copy).then_inc(h_copied, 1)
            act.wait_ge(weights_in, 16 * n_weights)
            for n, (k0, kn) in enumerate(s.chunks):
                act.wait_ge(z1_made, n + 1)
                at = (2 + n % 2) * BANK
                nc.scalar.activation(b.z1[:, k0 * T:(k0 + kn) * T], ps[:, at:at + kn * T], ACT.Identity,
                                     bias=b.vec[:, 0:1]).then_inc(z1_copied, 1)
            act.wait_ge(var_1, 1)
            nc.scalar.activation(b.mv[:, 2:3], b.mv[:, 1:2], ACT.Sqrt, bias=b.epst[:, :]).then_inc(std_1, 1)
            act.wait_ge(bn1_made, 1)
            for n, (k0, kn) in enumerate(s.chunks):
                z = b.z1[:, k0 * T:(k0 + kn) * T]
                nc.scalar.activation(z, z, ACT.Relu, bias=b.mv[:, 6:7], scale=b.mv[:, 4:5]).then_inc(a1_made, 1)
            for n, (k0, kn) in enumerate(s.chunks):
                act.wait_ge(z2_made, n + 1)
                at = (4 + n % 2) * BANK
                nc.scalar.activation(b.hT[:, k0 * T:(k0 + kn) * T], ps[0:D, at:at + kn * T], ACT.Identity,
                                     bias=b.vec[0:D, 3:4]).then_inc(z2_copied, 1)
            nc.scalar.activation(b.vabs[:, :], b.Vt[0:D, :], ACT.Abs).then_inc(abs_made, 1)
            act.wait_ge(var_2, 1)
            nc.scalar.activation(b.mv[0:D, 2:3], b.mv[0:D, 1:2], ACT.Sqrt, bias=b.epst[0:D, :]).then_inc(std_2, 1)
            act.wait_ge(bn2_made, 1)
            for n, (k0, kn) in enumerate(s.chunks):
                z = b.hT[:, k0 * T:(k0 + kn) * T]
                nc.scalar.activation(z, z, ACT.Relu, bias=b.mv[0:D, 6:7], scale=b.mv[0:D, 4:5]).then_inc(a2_made, 1)
            layernorm_root(nc, act, s, b, b.stc, var_c, std_c)

        @block.vector
        def _(dve):
            chain = Chain(dve, dve_own)
            link = chain.link
            dve.wait_ge(eps_wide, 1)
            link(nc.vector.tensor_scalar(b.ep1[:, 1:2], ps[0:T, 7 * BANK + G:7 * BANK + G + 1], 1.0, None, ALU.add))
            dve.sem_inc(eps_used, 1)
            dve.wait_ge(h_in, 16)
            for j in range(s.NB):
                dve.wait_ge(raw_in[j % 2], 16 * (j // 2 + 1))
                r3 = raw[j % 2][:, :].rearrange("p (u c) -> p u c", c=RAW)
                t3, hj = tiles3(b.tmp[:, :], D), b.hc[:, j * TB * D:(j + 1) * TB * D]
                deg = b.stc[:, 0:TB]
                link(nc.vector.tensor_scalar(deg, r3[:, :, 5 * D], 1.0, None, ALU.max))
                link(nc.vector.reciprocal(deg, deg))
                link(nc.vector.tensor_tensor(t3, r3[:, :, 3 * D:4 * D], r3[:, :, 4 * D:5 * D], ALU.add))
                link(nc.vector.scalar_tensor_tensor(t3, t3, 1.0 / HSCALE, r3[:, :, 0:D], ALU.mult, ALU.add))
                link(nc.vector.tensor_tensor(t3, t3, r3[:, :, D:2 * D], ALU.add))
                link(nc.vector.tensor_tensor(t3, t3, r3[:, :, 2 * D:3 * D], ALU.add))
                dve.sem_inc(raw_used, 1)
                link(nc.vector.tensor_tensor(t3, t3, wide(deg, D), ALU.mult))
                link(nc.vector.scalar_tensor_tensor(hj, hj, b.ep1[:, 1:2], b.tmp[:, :], ALU.mult, ALU.add))
            dve.sem_inc(hcat_made, 1)
            dve.wait_ge(deg_turned, 1)
            deg = ps[0:T, 7 * BANK:7 * BANK + G]
            link(nc.vector.tensor_scalar(b.stc[:, 0:G], deg, 1.0, None, ALU.max))
            dve.sem_inc(deg_safe, 1)
            nc.vector.tensor_reduce(b.growth[:, :], b.stc[:, 0:G], AX.X, ALU.max).then_inc(deg_max, 1)
            link(nc.vector.tensor_scalar(b.stc[:, 2 * G:3 * G], deg, 0.5, None, ALU.is_gt))
            dve.wait_ge(deg_root, 1)
            link(nc.vector.reciprocal(b.dinv[:, :], b.stc[:, G:2 * G]))
            link(nc.vector.tensor_tensor(b.dinv[:, :], b.dinv[:, :], b.stc[:, 2 * G:3 * G], ALU.mult))
            for n, (k0, kn) in enumerate(s.chunks):
                dve.wait_ge(z1_copied, n + 1)
                link(nc.vector.bn_stats(b.stats[:, 6 * n:6 * n + 6], b.z1[:, k0 * T:(k0 + kn) * T]))
            batchnorm_dve(nc, dve, link, b, P, 0, var_1, std_1, bn1_made)
            dve.wait_ge(a1_made, NCH)
            for n, (k0, kn) in enumerate(s.chunks):
                dve.wait_ge(z2_copied, n + 1)
                link(nc.vector.bn_stats(b.stats[0:D, 6 * n:6 * n + 6], b.hT[:, k0 * T:(k0 + kn) * T]))
            batchnorm_dve(nc, dve, link, b, D, 3, var_2, std_2, bn2_made)
            dve.wait_ge(x_in, 16)
            for n, (k0, kn) in enumerate(s.chunks):
                dve.wait_ge(a2_turned, n + 1)
                xj = b.hc[:, k0 * D:(k0 + kn) * D]
                link(nc.vector.tensor_tensor(xj, xj, ps[0:T, (n % 2) * BANK:(n % 2) * BANK + kn * D], ALU.add))
                dve.sem_inc(a2_used, 1)
            layernorm(nc, dve, chain, s, b.hc, b.xcc, b.sqc, b.stc, b.hN, var_c, std_c)
            link(nc.vector.tensor_tensor(b.hc[:, :], b.hc[:, :], b.hN[:, :], ALU.add))
            dve.sem_inc(res_made, 1)
            dve.wait_ge(omega_summed, 1)
            for layer in range(3):
                link(nc.vector.tensor_reduce(b.omega[:, layer * K:(layer + 1) * K],
                                             tiles3(ps[0:T, (2 + layer) * BANK:(2 + layer) * BANK + K * D], D),
                                             AX.X, ALU.max))
            dve.wait_ge(growth_made, 1)


def chebyshev_phase(nc, s, b, A, sem):
    N, G, D, K, NCH = s.N, s.G, s.D, s.K, s.NCH
    ps = b.ps
    ones_set, jj_made, bias_set = sem("ones_set"), sem("jj_made"), sem("bias_set")
    h_turned, h_copied, x_made = sem("x_turned"), sem("x_copied"), sem("layer_input")
    main_made, main_copied, combined, comb_used = sem("main_made"), sem("main_copied"), sem("combined"), sem("comb_used")
    parts_made, max_made, max_all = sem("parts_made"), sem("max_made"), sem("max_all")
    dve_own, waited = sem("dve_own_d"), sem("waited_d")
    vs, tb = (b.vs0, b.vs1), (b.tb0, b.tb1)
    bs = (b.hN, b.bB)
    R = K
    MB, CB = 0, 4
    free = min([4] * (NCH > 4) + [NCH + n - c for n in range(NCH) for c in range(NCH)
                                  if n % 4 == c % 4 and c - n < NCH])

    def rounds(engine, layer, one):
        one(layer, 0, 0)
        with engine.Fori(0, (R - 2) // 2) as t:
            one(layer, 1 + 2 * t, 1)
            one(layer, 2 + 2 * t, 0)
        one(layer, R - 1, 1)

    def is_first(r):
        return isinstance(r, int) and r == 0

    def is_last(r):
        return isinstance(r, int) and r == R - 1

    with nc.Block() as block:
        @block.gpsimd
        def _(pool):
            nc.gpsimd.memset(b.hTc[D:D + 1, :], 1.0).then_inc(ones_set, 1)
            pool.wait_ge(ones_set, 1)
            with pool.Fori(0, 3) as layer:
                with pool.Fori(0, R) as r:
                    n = layer * R + r
                    pool.wait_ge(max_made, n + 1)
                    pool.sem_inc(waited, 1)
                    nc.gpsimd.partition_all_reduce(b.mx[:, 1:2], b.mx[:, 0:1], T, RMAX).then_inc(max_all, 1)

        @block.tensor
        def _(pe):
            pe.wait_ge(ones_set, 1)
            pe.wait_ge(jj_made, 2)

            def turn_input(layer):
                pe.wait_ge(x_made, layer + 1)
                for n, (k0, kn) in enumerate(s.chunks):
                    if n >= 4:
                        pe.wait_ge(h_copied, layer * NCH + (n - 3))
                    for k in range(kn):
                        at = (MB + n % 4) * BANK + k * T
                        last = nc.tensor.matmul(ps[0:D, at:at + T], b.hN[:, (k0 + k) * D:(k0 + k + 1) * D],
                                                b.identf[0:T, 0:T], start=True, stop=True)
                    last.then_inc(h_turned, 1)

            def one(layer, r, odd):
                weights = layer * (K * D) + r * D

                def main(n):
                    k0, kn = s.chunks[n]
                    count = (layer * (R - 1) + (r - 1)) * NCH + n
                    pe.wait_ge(main_copied, count + 1)
                    for k in range(G):
                        if n == 0 and k % CHUNK == 0:
                            pe.wait_ge(parts_made, (layer * (R - 1) + (r - 1)) * NCH + k // CHUNK + 1)
                        at = (MB + n % 4) * BANK
                        last = nc.tensor.matmul(ps[:, at:at + kn * T], vs[1 - odd][:, k * 2 * D:(k + 1) * 2 * D],
                                                b.C[:, k * N + k0 * T:k * N + (k0 + kn) * T], start=(k == 0),
                                                stop=(k == G - 1))
                    last.then_inc(main_made, 1)

                def combine(n):
                    k0, kn = s.chunks[n]
                    done = (layer * R + r) * NCH + n
                    at = (CB + n % 4) * BANK
                    pe.wait_ge(comb_used, done + 1)
                    if is_first(r):
                        pe.wait_ge(h_copied, layer * NCH + (n + 1))
                    for k in range(kn):
                        last = nc.tensor.matmul(
                            ps[0:T, at + CHUNK * D + k * D:at + CHUNK * D + (k + 1) * D],
                            b.hTc[:, (k0 + k) * T:(k0 + k + 1) * T],
                            b.Vt[:, ds(weights, D)], start=True, stop=True)
                    if not is_first(r):
                        pe.wait_ge(main_copied, (layer * (R - 1) + (r - 1)) * NCH + (n + 1 + free))
                        for k in range(kn):
                            last = nc.tensor.matmul(ps[0:T, at + k * D:at + (k + 1) * D],
                                                    tb[n % 2][:, k * T:(k + 1) * T], b.JJ[:, :], start=True,
                                                    stop=True)
                    last.then_inc(combined, 1)

                if is_first(r):
                    for n in range(NCH):
                        combine(n)
                else:
                    main(0)
                    for n in range(1, NCH):
                        main(n)
                        combine(n - 1)
                    combine(NCH - 1)

            pe.sem_inc(comb_used, free)
            pe.sem_inc(main_copied, free)
            with pe.Fori(0, 3) as layer:
                turn_input(layer)
                rounds(pe, layer, one)

        @block.scalar
        def _(act):
            def one(layer, r, odd):
                if is_first(r):
                    return
                for n, (k0, kn) in enumerate(s.chunks):
                    act.wait_ge(main_made, (layer * (R - 1) + (r - 1)) * NCH + n + 1)
                    act.wait_ge(combined, (layer * R + r) * NCH + max(n - 1, 0))
                    at = (MB + n % 4) * BANK
                    nc.scalar.activation(tb[n % 2][:, 0:kn * T], ps[:, at:at + kn * T], ACT.Copy).then_inc(
                        main_copied, 1)

            with act.Fori(0, 3) as layer:
                for n, (k0, kn) in enumerate(s.chunks):
                    act.wait_ge(h_turned, layer * NCH + (n + 1))
                    at = (MB + n % 4) * BANK
                    nc.scalar.activation(b.hTc[0:D, k0 * T:(k0 + kn) * T], ps[0:D, at:at + kn * T],
                                         ACT.Copy).then_inc(h_copied, 1)
                rounds(act, layer, one)

        @block.vector
        def _(dve):
            chain = Chain(dve, dve_own)
            link = chain.link
            nc.vector.tensor_copy(b.JJ[0:D, :], b.identf[0:D, 0:D]).then_inc(jj_made, 1)
            nc.vector.tensor_copy(b.JJ[D:2 * D, :], b.identf[D:2 * D, D:2 * D]).then_inc(jj_made, 1)
            hmax, new, old, bound, t0 = (b.sc[:, k:k + 1] for k in range(5))
            before, in_first, in_mid, in_last = 3, 3 * NCH + 7, 5 * NCH + 10, 3 * NCH + 2
            in_layer = before + in_first + (R - 2) * in_mid + in_last

            def one(layer, r, odd):
                target, first_round, last_round = bs[odd], is_first(r), is_last(r)
                done = (layer * R + r) * NCH
                chain.turn(layer * in_layer + before + (0 if first_round else in_first + (r - 1) * in_mid))
                column = layer * K + r
                if not first_round:
                    link(nc.vector.tensor_scalar(t0, bound, (-1.0 if last_round else -2.0) / TOP, None, ALU.mult))
                    link(nc.vector.tensor_scalar(b.gv[:, :], b.dinv[:, :], t0, None, ALU.mult))
                for n, (k0, kn) in enumerate(s.chunks):
                    at = (CB + n % 4) * BANK
                    w = kn * D
                    prop, lin = ps[0:T, at:at + w], ps[0:T, at + CHUNK * D:at + CHUNK * D + w]
                    ua, ub = (b.ua0, b.ua1)[n % 2][:, 0:w], b.ub[:, 0:w]
                    to = target[:, k0 * D:(k0 + kn) * D]
                    dve.wait_ge(combined, done + (n + 1))
                    if first_round:
                        nc.vector.tensor_copy(to, lin).then_inc(comb_used, 1)
                        dve.wait_ge(comb_used, done + (n + 1 + free))
                    else:
                        link(nc.vector.tensor_tensor(tiles3(ua, D), tiles3(prop, D), wide(b.gv[:, k0:k0 + kn], D),
                                                     ALU.mult))
                        nc.vector.tensor_tensor(ub, lin, to, ALU.subtract).then_inc(comb_used, 1)
                        dve.wait_ge(comb_used, done + (n + 1 + free))
                        if last_round:
                            link(nc.vector.tensor_tensor(ua, ua, ub, ALU.add))
                            link(nc.vector.tensor_scalar(b.hN[:, k0 * D:(k0 + kn) * D], ua, 0.0, None, ALU.max))
                            continue
                        link(nc.vector.tensor_tensor(to, ua, ub, ALU.add))
                    link(nc.vector.tensor_reduce(b.mxp[:, n:n + 1], to, AX.X, ALU.max, apply_absolute_value=True))
                    if n == 0:
                        dve.wait_ge(max_all, layer * R + r + 1)
                        if first_round:
                            link(nc.vector.tensor_copy(hmax, b.mx[:, 1:2]))
                        else:
                            link(nc.vector.tensor_copy(old, new))
                            link(nc.vector.tensor_copy(new, b.mx[:, 1:2]))
                        om = b.omega[:, ds(column, 1)]
                        link(nc.vector.tensor_tensor(bound, om, hmax, ALU.mult))
                        link(nc.vector.tensor_tensor(bound, bound, old, ALU.add))
                        link(nc.vector.scalar_tensor_tensor(bound, new, b.growth[:, :], bound, ALU.mult, ALU.add))
                        link(nc.vector.tensor_scalar(bound, bound, 1e-20, None, ALU.max))
                        link(nc.vector.reciprocal(t0, bound))
                        link(nc.vector.tensor_scalar(b.av[:, :], b.dinv[:, :], t0, TOP, ALU.mult, ALU.mult))
                    parts = tiles3(vs[odd][:, k0 * 2 * D:(k0 + kn) * 2 * D], 2 * D)
                    link(nc.vector.tensor_tensor(tiles3(ua, D), tiles3(to, D), wide(b.av[:, k0:k0 + kn], D),
                                                 ALU.mult))
                    link(nc.vector.tensor_copy(parts[:, :, 0:D], tiles3(ua, D)))
                    nc.vector.tensor_tensor(parts[:, :, D:2 * D], tiles3(ua, D), parts[:, :, 0:D],
                                            ALU.subtract).then_inc(parts_made, 1)
                if last_round:
                    assert chain.n == in_last
                    dve.wait_ge(max_all, layer * R + R)
                else:
                    assert chain.n == (in_first if first_round else in_mid)
                    nc.vector.tensor_reduce(b.mx[:, 0:1], b.mxp[:, 0:NCH], AX.X, ALU.max).then_inc(max_made, 1)

            with dve.Fori(0, 3) as layer:
                dve.sem_inc(x_made, 1)
                chain.turn(layer * in_layer)
                nc.vector.tensor_reduce(b.mx[:, 0:1], b.hN[:, :], AX.X, ALU.max).then_inc(max_made, 1)
                link(nc.vector.memset(b.bB[:, :], 0.0))
                link(nc.vector.memset(new, 0.0))
                link(nc.vector.memset(old, 0.0))
                assert chain.n == before
                rounds(dve, layer, one)


def output_phase(nc, s, b, A, sem):
    res_in, out_made, out_stored = sem("res_in"), sem("out_made"), sem("out_stored")
    with nc.Block() as block:
        @block.sync
        def _(sp):
            sp.dma_start(b.bB[:, :], b.res_dram).then_inc(res_in, 16)
            sp.wait_ge(out_made, 1)
            sp.dma_start(A.out.rearrange("(i p) c -> p i c", p=T), tiles3(b.bB[:, :], s.D)).then_inc(out_stored, 16)
            sp.wait_ge(out_stored, 16)

        @block.vector
        def _(dve):
            dve.wait_ge(res_in, 16)
            nc.vector.tensor_tensor(b.bB[:, :], b.bB[:, :], b.hN[:, :], ALU.add).then_inc(out_made, 1)


def gnn_kernel(nc, x, src, dst, edge_attr, eps, W1, b1, gamma1, beta1, W2, b2, gamma2, beta2,
               V1, c1, V2, c2, V3, c3, out):
    A = record(x=x, src=src, dst=dst, edge_attr=edge_attr, eps=eps, W1=W1, b1=b1, gamma1=gamma1,
                        beta1=beta1, W2=W2, b2=b2, gamma2=gamma2, beta2=beta2, V1=V1, c1=c1, V2=V2, c2=c2,
                        V3=V3, c3=c3, out=out)
    s = shapes_of(x.shape[0], src.shape[0], x.shape[1], W1.shape[1], V1.shape[0])
    with ExitStack() as ctx:
        b = place(nc, s, ctx)

        def sem(name):
            return ctx.enter_context(nc.semaphore(name))

        keys_phase(nc, s, b, A, sem)
        counts_phase(nc, s, b, A, sem)
        perceptron_phase(nc, s, b, A, sem)
        chebyshev_phase(nc, s, b, A, sem)
        output_phase(nc, s, b, A, sem)


_INS = ["x", "src", "dst", "edge_attr_64", "L0_gnn_eps", "L0_gnn_W1", "L0_gnn_b1", "L0_gnn_gamma1", "L0_gnn_beta1",
        "L0_gnn_W2", "L0_gnn_b2", "L0_gnn_gamma2", "L0_gnn_beta2", "L1_gnn_W1", "L1_gnn_b1", "L1_gnn_W2", "L1_gnn_b2",
        "L1_gnn_W3", "L1_gnn_b3"]


def kernel(**inputs):
    import numpy as _np
    import concourse.bacc as _bacc
    from concourse import mybir as _mybir
    from concourse.bass_utils import run_bass_kernel_spmd as _run

    nc = _bacc.Bacc("TRN2", target_bir_lowering=False, num_devices=1)
    arrays, args = {}, []
    for name in _INS:
        a = _np.ascontiguousarray(inputs[name])
        arrays[f"in_{name}_dram"] = a
        args.append(nc.dram_tensor(f"in_{name}_dram", a.shape, _mybir.dt.from_np(a.dtype), kind="ExternalInput").ap())
    shape = inputs["x"].shape
    args.append(nc.dram_tensor("out_0_dram", shape, _mybir.dt.float32, kind="ExternalOutput").ap())
    gnn_kernel(nc, *args)
    r = _run(nc, [arrays], core_ids=[0])
    return r.results[0]["out_0_dram"]
```
